# Optimizing a Trainium2 kernel written in Bass

```python
import numpy as np
import jax
import jax.numpy as jnp

def _softmax(x, axis=-1):
    return jax.nn.softmax(x, axis=axis)

def _gelu(x):
    return jax.nn.gelu(x, approximate=True)

def _silu(x):
    return jax.nn.silu(x)

def _sigmoid(x):
    return jax.nn.sigmoid(x)

def _layernorm(x, axis=-1, eps=1e-05):
    m = jnp.mean(x, axis=axis, keepdims=True)
    v = jnp.var(x, axis=axis, keepdims=True)
    return (x - m) / jnp.sqrt(v + eps)

def _scatter_add(tgt, idx, src, axis=0):
    return tgt.at[idx].add(src)

def _segment_sum(src, seg, n):
    return jax.ops.segment_sum(src, seg, n)
kernel_name = 'mk_dlrm_tower_d1_rec_r8_de96ea'

def setup_inputs(seed: int=0):
    np.random.seed(seed)
    _w = jnp.asarray

    def _rec_inputs():
        import jax
        import jax.numpy as jnp
        _tk = jax.random.key(seed)
        ids = jnp.stack([jax.random.randint(jax.random.fold_in(_tk, 200 + f), (512,), 0, v, jnp.int32) for f, v in enumerate([1000, 125000, 1250, 1250, 1250, 1250, 1000, 1250, 1250, 1250, 12500, 1000, 12500, 1250, 1000, 1250, 1000, 12500, 1000, 1250, 1000, 12500, 12500, 1250, 1000, 12500])], axis=1)
        tbl_0 = 0.05 * jax.random.normal(jax.random.fold_in(_tk, 500 + 0), (1000, 128), jnp.float32)
        tbl_1 = 0.05 * jax.random.normal(jax.random.fold_in(_tk, 500 + 1), (125000, 128), jnp.float32)
        tbl_2 = 0.05 * jax.random.normal(jax.random.fold_in(_tk, 500 + 2), (1250, 128), jnp.float32)
        tbl_3 = 0.05 * jax.random.normal(jax.random.fold_in(_tk, 500 + 3), (1250, 128), jnp.float32)
        tbl_4 = 0.05 * jax.random.normal(jax.random.fold_in(_tk, 500 + 4), (1250, 128), jnp.float32)
        tbl_5 = 0.05 * jax.random.normal(jax.random.fold_in(_tk, 500 + 5), (1250, 128), jnp.float32)
        tbl_6 = 0.05 * jax.random.normal(jax.random.fold_in(_tk, 500 + 6), (1000, 128), jnp.float32)
        tbl_7 = 0.05 * jax.random.normal(jax.random.fold_in(_tk, 500 + 7), (1250, 128), jnp.float32)
        tbl_8 = 0.05 * jax.random.normal(jax.random.fold_in(_tk, 500 + 8), (1250, 128), jnp.float32)
        tbl_9 = 0.05 * jax.random.normal(jax.random.fold_in(_tk, 500 + 9), (1250, 128), jnp.float32)
        tbl_10 = 0.05 * jax.random.normal(jax.random.fold_in(_tk, 500 + 10), (12500, 128), jnp.float32)
        tbl_11 = 0.05 * jax.random.normal(jax.random.fold_in(_tk, 500 + 11), (1000, 128), jnp.float32)
        tbl_12 = 0.05 * jax.random.normal(jax.random.fold_in(_tk, 500 + 12), (12500, 128), jnp.float32)
        tbl_13 = 0.05 * jax.random.normal(jax.random.fold_in(_tk, 500 + 13), (1250, 128), jnp.float32)
        tbl_14 = 0.05 * jax.random.normal(jax.random.fold_in(_tk, 500 + 14), (1000, 128), jnp.float32)
        tbl_15 = 0.05 * jax.random.normal(jax.random.fold_in(_tk, 500 + 15), (1250, 128), jnp.float32)
        tbl_16 = 0.05 * jax.random.normal(jax.random.fold_in(_tk, 500 + 16), (1000, 128), jnp.float32)
        tbl_17 = 0.05 * jax.random.normal(jax.random.fold_in(_tk, 500 + 17), (12500, 128), jnp.float32)
        tbl_18 = 0.05 * jax.random.normal(jax.random.fold_in(_tk, 500 + 18), (1000, 128), jnp.float32)
        tbl_19 = 0.05 * jax.random.normal(jax.random.fold_in(_tk, 500 + 19), (1250, 128), jnp.float32)
        tbl_20 = 0.05 * jax.random.normal(jax.random.fold_in(_tk, 500 + 20), (1000, 128), jnp.float32)
        tbl_21 = 0.05 * jax.random.normal(jax.random.fold_in(_tk, 500 + 21), (12500, 128), jnp.float32)
        tbl_22 = 0.05 * jax.random.normal(jax.random.fold_in(_tk, 500 + 22), (12500, 128), jnp.float32)
        tbl_23 = 0.05 * jax.random.normal(jax.random.fold_in(_tk, 500 + 23), (1250, 128), jnp.float32)
        tbl_24 = 0.05 * jax.random.normal(jax.random.fold_in(_tk, 500 + 24), (1000, 128), jnp.float32)
        tbl_25 = 0.05 * jax.random.normal(jax.random.fold_in(_tk, 500 + 25), (12500, 128), jnp.float32)
        _rk = jax.random.fold_in(_tk, 7)
        r_bottom_output = -0.000520686 + 1.00062 * jax.random.normal(jax.random.fold_in(_rk, 101), (512, 128), jnp.float32)
        W_top1 = 0.0456912 * jax.random.normal(jax.random.fold_in(_tk, 801), (479, 512), jnp.float32)
        W_top2 = 0.0441942 * jax.random.normal(jax.random.fold_in(_tk, 802), (512, 256), jnp.float32)
        W_top3 = 0.0625 * jax.random.normal(jax.random.fold_in(_tk, 803), (256, 1), jnp.float32)
        b_top1 = jnp.zeros((512,), jnp.float32)
        b_top2 = jnp.zeros((256,), jnp.float32)
        return (r_bottom_output, ids, tbl_0, tbl_1, tbl_2, tbl_3, tbl_4, tbl_5, tbl_6, tbl_7, tbl_8, tbl_9, tbl_10, tbl_11, tbl_12, tbl_13, tbl_14, tbl_15, tbl_16, tbl_17, tbl_18, tbl_19, tbl_20, tbl_21, tbl_22, tbl_23, tbl_24, tbl_25, W_top1, b_top1, W_top2, b_top2, W_top3)
    r_bottom_output, ids, tbl_0, tbl_1, tbl_2, tbl_3, tbl_4, tbl_5, tbl_6, tbl_7, tbl_8, tbl_9, tbl_10, tbl_11, tbl_12, tbl_13, tbl_14, tbl_15, tbl_16, tbl_17, tbl_18, tbl_19, tbl_20, tbl_21, tbl_22, tbl_23, tbl_24, tbl_25, W_top1, b_top1, W_top2, b_top2, W_top3 = _rec_inputs()

    def _L0_rec_setup():
        import jax, jax.numpy as jnp
        import numpy as np
        NUM_FEATURES = 27
        _TRIU_I, _TRIU_J = np.triu_indices(NUM_FEATURES, k=1)
        key = jax.random.key(seed)
        k1, k2 = jax.random.split(key)
        bottom_output = jax.random.normal(k1, (2048, 128), dtype=jnp.float32)
        embeddings = jax.random.normal(k2, (2048, 26, 128), dtype=jnp.float32)
        return {'bottom_output': bottom_output, 'embeddings': embeddings}
    _L0_rec_all = _L0_rec_setup()
    _L0_rec_in = {k: v for k, v in _L0_rec_all.items() if k in ()}
    del _L0_rec_all
    return {'r_bottom_output': r_bottom_output, 'ids': ids, 'tbl_0': tbl_0, 'tbl_1': tbl_1, 'tbl_2': tbl_2, 'tbl_3': tbl_3, 'tbl_4': tbl_4, 'tbl_5': tbl_5, 'tbl_6': tbl_6, 'tbl_7': tbl_7, 'tbl_8': tbl_8, 'tbl_9': tbl_9, 'tbl_10': tbl_10, 'tbl_11': tbl_11, 'tbl_12': tbl_12, 'tbl_13': tbl_13, 'tbl_14': tbl_14, 'tbl_15': tbl_15, 'tbl_16': tbl_16, 'tbl_17': tbl_17, 'tbl_18': tbl_18, 'tbl_19': tbl_19, 'tbl_20': tbl_20, 'tbl_21': tbl_21, 'tbl_22': tbl_22, 'tbl_23': tbl_23, 'tbl_24': tbl_24, 'tbl_25': tbl_25, 'W_top1': W_top1, 'b_top1': b_top1, 'W_top2': W_top2, 'b_top2': b_top2, 'W_top3': W_top3}

def reference(r_bottom_output, ids, tbl_0, tbl_1, tbl_2, tbl_3, tbl_4, tbl_5, tbl_6, tbl_7, tbl_8, tbl_9, tbl_10, tbl_11, tbl_12, tbl_13, tbl_14, tbl_15, tbl_16, tbl_17, tbl_18, tbl_19, tbl_20, tbl_21, tbl_22, tbl_23, tbl_24, tbl_25, W_top1, b_top1, W_top2, b_top2, W_top3):
    import jax
    import jax.numpy as jnp

    def _L0_rec_ref(bottom_output, embeddings):
        import jax, jax.numpy as jnp
        import numpy as np
        NUM_FEATURES = 27
        _TRIU_I, _TRIU_J = np.triu_indices(NUM_FEATURES, k=1)
        all_emb = jnp.concatenate([bottom_output[:, None, :], embeddings], axis=1)
        gram = jnp.einsum('bfd,bgd->bfg', all_emb, all_emb)
        return gram[:, _TRIU_I, _TRIU_J]
    e = jnp.stack([tbl_0[ids[:, 0]], tbl_1[ids[:, 1]], tbl_2[ids[:, 2]], tbl_3[ids[:, 3]], tbl_4[ids[:, 4]], tbl_5[ids[:, 5]], tbl_6[ids[:, 6]], tbl_7[ids[:, 7]], tbl_8[ids[:, 8]], tbl_9[ids[:, 9]], tbl_10[ids[:, 10]], tbl_11[ids[:, 11]], tbl_12[ids[:, 12]], tbl_13[ids[:, 13]], tbl_14[ids[:, 14]], tbl_15[ids[:, 15]], tbl_16[ids[:, 16]], tbl_17[ids[:, 17]], tbl_18[ids[:, 18]], tbl_19[ids[:, 19]], tbl_20[ids[:, 20]], tbl_21[ids[:, 21]], tbl_22[ids[:, 22]], tbl_23[ids[:, 23]], tbl_24[ids[:, 24]], tbl_25[ids[:, 25]]], axis=1)
    z = _L0_rec_ref(r_bottom_output, e)
    z = z.reshape(z.shape[0], -1)
    h = jnp.concatenate([z, r_bottom_output], axis=1)
    h = jnp.maximum(h @ W_top1 + b_top1, 0.0)
    h = jnp.maximum(h @ W_top2 + b_top2, 0.0)
    y = h @ W_top3
    return y

_drawn_inputs = setup_inputs


def setup_inputs(seed=0):
    import zlib

    import numpy as np

    out = dict(_drawn_inputs(seed))
    spreads = {'b_top1': (0.0, 0.1), 'b_top2': (0.0, 0.1)}
    factors = {}
    for name, (base, spread) in spreads.items():
        noise = np.random.default_rng([zlib.crc32(name.encode()), seed]).standard_normal(out[name].shape)
        drawn = base * np.exp(spread * noise) if base else spread * noise
        out[name] = jnp.asarray(drawn.astype(out[name].dtype))
    for name, factor in factors.items():
        out[name] = (out[name] * factor).astype(out[name].dtype)
    return out
```

```python
from contextlib import ExitStack

import concourse.bass as bass
from concourse import mybir

F32 = mybir.dt.float32
I32 = mybir.dt.int32
ALU = mybir.AluOpType
ACT = mybir.ActivationFunctionType

P = 128
Q = 32
NQ = P // Q
BATCH = 512
BLOCKS = BATCH // P
D = 128
TABLES = 26
FEATS = TABLES + 1
KPAIR = (FEATS - 1) // 2
PAIRS = FEATS * KPAIR
ZCH = 3
ZROWS = PAIRS // ZCH
H1, H2 = 512, 256
N1, N2 = H1 // P, H2 // P
CHUNK = 4
CHUNKS = [range(c, min(c + CHUNK, TABLES)) for c in range(0, TABLES, CHUNK)]
EVEN, ODD = (len(CHUNKS) + 1) // 2, len(CHUNKS) // 2
BANK = 512
GPB = 4
SPAN = 2 * GPB
SPANS = Q // SPAN


KS = [(1, 6), (6, 10), (10, 14)]


def pair_rows():
    rows = []
    for k in range(1, KPAIR + 1):
        for f in range(FEATS):
            a, b = sorted((f, (f + k) % FEATS))
            rows.append(a * FEATS - a * (a + 1) // 2 + b - a - 1)
    return rows


def build(nc, ids, bottom, tables, w1_pairs, w1_bottom, b1, w2, b2, w3, out):
    with ExitStack() as ctx:
        def sb(name, shape, dt=F32):
            return ctx.enter_context(nc.sbuf_tensor(name, shape, dt))

        def psum(name, shape):
            return ctx.enter_context(nc.psum_tensor(name, shape, F32))

        def sem(name):
            return ctx.enter_context(nc.semaphore(name))

        ids_sb = sb("ids_sb", [P, BLOCKS, TABLES], I32)
        bottom_sb = sb("bottom_sb", [P, BLOCKS, D])
        w1p_sb = sb("w1p_sb", [ZROWS, ZCH, H1])
        w1b_sb = sb("w1b_sb", [P, H1])
        w2_sb = sb("w2_sb", [P, N1, H2])
        w3_sb = sb("w3_sb", [P, N2])
        b1_sb = sb("b1_sb", [P, N1])
        b2_sb = sb("b2_sb", [P, N2])
        ident = sb("ident", [P, P])
        emb = sb("emb", [P, TABLES, D])
        bottomT = sb("bottomT", [P, BATCH])
        featT = sb("featT", [P, Q, NQ, Q])
        gram = sb("gram", [P, Q, FEATS])
        gramT = sb("gramT", [P, FEATS + KPAIR, Q])
        pairs = sb("pairs", [P, PAIRS])
        pairsT = sb("pairsT", [ZROWS, ZCH, P])
        h1T = sb("h1T", [P, N1, P])
        h2T = sb("h2T", [P, N2, P])
        y_sb = sb("y_sb", [1, BATCH])

        psT = [psum(f"psT{i}", [P, CHUNK, P]) for i in range(2)]
        psG = [psum(f"psG{i}", [P, 2, BANK]) for i in range(2)]
        psZ = psum("psZ", [P, 4, P])
        psM = psum("psM", [P, 4, P])

        ids_in = sem("ids_in")
        bottom_in = sem("bottom_in")
        weights_in = sem("weights_in")
        ident_zero = sem("ident_zero")
        ident_ready = sem("ident_ready")
        pad_ready = sem("pad_ready")
        gathered = [sem(f"gathered{f}") for f in range(TABLES)]
        transposed = [sem(f"transposed{c}") for c in range(len(CHUNKS))]
        bottomT_done = sem("bottomT_done")
        bottomT_ready = sem("bottomT_ready")
        featT_even = sem("featT_even")
        featT_odd = sem("featT_odd")
        featT_bottom = sem("featT_bottom")
        gram_done = sem("gram_done")
        gram_act = sem("gram_act")
        gram_dve = sem("gram_dve")
        gramT_ready = sem("gramT_ready")
        pairs_act = sem("pairs_act")
        pairs_dve = sem("pairs_dve")
        pairsT_done = sem("pairsT_done")
        pairsT_act = sem("pairsT_act")
        pairsT_dve = sem("pairsT_dve")
        h1_done = sem("h1_done")
        h1_act = sem("h1_act")
        h1_dve = sem("h1_dve")
        h2_done = sem("h2_done")
        h2_act = sem("h2_act")
        h2_dve = sem("h2_dve")
        y_done = sem("y_done")
        y_ready = sem("y_ready")
        out_written = sem("out_written")

        WEIGHT_DMAS = 6

        def gram_block(span, j):
            return psG[span % 2][Q * j:Q * (j + 1), :, 0:GPB * NQ * FEATS].rearrange(
                "p b (i s) -> p b i s", i=GPB)[:, :, :, j * FEATS:(j + 1) * FEATS]

        def gram_to(span, j):
            return gram[Q * j:Q * (j + 1), span * SPAN:(span + 1) * SPAN, :].rearrange(
                "p (b i) g -> p b i g", b=2)

        def featT_cols(c):
            return featT[:].rearrange("p i j f -> p (i j) f")[:, :, 1 + CHUNKS[c].start:1 + CHUNKS[c].stop]

        def psT_cols(c):
            return psT[c % 2][:, 0:len(CHUNKS[c]), :].rearrange("p f s -> p s f")

        def band(k0, k1):
            return bass.AP(gramT, k0 * Q, [[(FEATS + KPAIR) * Q, P], [Q, k1 - k0], [Q + 1, FEATS]])

        def pairs_to(k0, k1):
            return pairs[:, k0 * FEATS - FEATS:k1 * FEATS - FEATS].rearrange("p (k f) -> p k f", f=FEATS)

        block = ctx.enter_context(nc.Block())

        @block.sync
        def _(sp):
            sp.dma_start(ids_sb[:], ids.rearrange("(t p) f -> p t f", p=P)).then_inc(ids_in, 16)
            sp.dma_start(bottom_sb[:], bottom.rearrange("(t p) d -> p t d", p=P)).then_inc(bottom_in, 16)
            sp.dma_start(w1b_sb[:], w1_bottom).then_inc(weights_in, 16)
            sp.dma_start(w1p_sb[:], w1_pairs.rearrange("(c p) n -> p c n", c=ZCH)).then_inc(weights_in, 16)
            sp.dma_start(w2_sb[:], w2.rearrange("(c p) n -> p c n", c=N1)).then_inc(weights_in, 16)
            sp.dma_start(b1_sb[:], b1).then_inc(weights_in, 16)
            sp.dma_start(b2_sb[:], b2).then_inc(weights_in, 16)
            sp.dma_start(w3_sb[:], w3).then_inc(weights_in, 16)
            sp.wait_ge(y_ready, BLOCKS)
            sp.dma_start(out, y_sb[:]).then_inc(out_written, 16)
            sp.wait_ge(out_written, 16)

        @block.gpsimd
        def _(pool):
            nc.gpsimd.memset(ident[:], 0.0).then_inc(ident_zero, 1)
            pool.wait_ge(ident_zero, 1)
            nc.gpsimd.affine_select(out=ident[:], in_=ident[:], compare_op=ALU.not_equal, fill=1.0, base=0,
                                    pattern=[[-1, P]], channel_multiplier=1).then_inc(ident_ready, 1)
            pool.wait_ge(ids_in, 16)
            for t in range(BLOCKS):
                for c, chunk in enumerate(CHUNKS):
                    if t > 0:
                        pool.wait_ge(transposed[c], t)
                    for f in chunk:
                        if t > 0:
                            pool.wait_ge(gathered[f], 16 * t)
                        nc.gpsimd.indirect_dma_start(
                            out=emb[:, f, :], out_offset=None, in_=tables[f][:],
                            in_offset=bass.IndirectOffsetOnAxis(ap=ids_sb[:, t, f:f + 1], axis=0),
                        ).then_inc(gathered[f], 16)

        @block.tensor
        def _(pe):
            pe.wait_ge(ident_ready, 1)
            pe.wait_ge(bottom_in, 16)
            for b in range(BLOCKS):
                last = nc.tensor.transpose(psT[0][:, b, :], bottom_sb[:, b, :], ident[:])
            last.then_inc(bottomT_done, 1)
            pe.wait_ge(bottomT_ready, 1)
            pe.wait_ge(pad_ready, 1)
            pe.wait_ge(weights_in, 16 * WEIGHT_DMAS)
            with nc.tensor.Fori(0, BLOCKS) as t:
                for c, chunk in enumerate(CHUNKS):
                    if c >= 2 and c % 2 == 0:
                        pe.wait_ge(featT_even, EVEN * t + c // 2)
                    elif c >= 2:
                        pe.wait_ge(featT_odd, ODD * t + c // 2)
                    for n, f in enumerate(chunk):
                        pe.wait_ge(gathered[f], 16 * t + 16)
                        last = nc.tensor.transpose(psT[c % 2][:, n, :], emb[:, f, :], ident[:])
                    last.then_inc(transposed[c], 1)

                pe.wait_ge(featT_even, EVEN * t + EVEN)
                pe.wait_ge(featT_odd, ODD * t + ODD)
                pe.wait_ge(featT_bottom, t + 1)
                for s in range(SPANS):
                    if s >= 2:
                        pe.wait_ge(gram_act, SPANS * t + s - 1)
                        pe.wait_ge(gram_dve, SPANS * t + s - 1)
                    for n in range(SPAN):
                        i = s * SPAN + n
                        col = n % GPB * NQ * FEATS
                        last = nc.tensor.matmul(
                            psG[s % 2][:, n // GPB, col:col + NQ * FEATS],
                            featT[:, i, :, :], featT[:, i, :, 0:FEATS], start=True, stop=True)
                    last.then_inc(gram_done, 1)

                for n in range(N1):
                    if n % 2 == 0:
                        pe.wait_ge(gram_act, SPANS * t + SPANS - 1 + n // 2)
                        pe.wait_ge(gram_dve, SPANS * t + SPANS - 1 + n // 2)
                    nc.tensor.matmul(psG[n // 2][:, n % 2, 0:P], w1b_sb[:, n * P:(n + 1) * P],
                                     bottomT[:, bass.ts(t, P)], start=True, stop=False)

                for c in range(ZCH):
                    if c == 0:
                        pe.wait_ge(pairs_dve, 2 * t + 1)
                    elif c == 1:
                        pe.wait_ge(pairs_act, t + 1)
                    else:
                        pe.wait_ge(pairs_dve, 2 * t + 2)
                    dst = psM[0:ZROWS, 0, :] if c == 2 else psZ[0:ZROWS, c, :]
                    last = nc.tensor.transpose(dst, pairs[:, c * ZROWS:(c + 1) * ZROWS], ident[:])
                    if c > 0:
                        last.then_inc(pairsT_done, 1)

                pe.wait_ge(pairsT_dve, t + 1)
                pe.wait_ge(pairsT_act, t + 1)
                for n in range(N1):
                    for c in range(ZCH):
                        last = nc.tensor.matmul(psG[n // 2][:, n % 2, 0:P], w1p_sb[:, c, n * P:(n + 1) * P],
                                                pairsT[:, c, :], start=False, stop=(c == ZCH - 1))
                    last.then_inc(h1_done, 1)

                for c in range(N1):
                    if c % 2 == 0:
                        pe.wait_ge(h1_act, 2 * t + c // 2 + 1)
                    else:
                        pe.wait_ge(h1_dve, 2 * t + c // 2 + 1)
                    for m in range(N2):
                        last = nc.tensor.matmul((psM if m == 0 else psZ)[:, 0, :], w2_sb[:, c, m * P:(m + 1) * P],
                                                h1T[:, c, :], start=(c == 0), stop=(c == N1 - 1))
                        if c == N1 - 1:
                            last.then_inc(h2_done, 1)

                pe.wait_ge(h2_act, t + 1)
                pe.wait_ge(h2_dve, t + 1)
                for c in range(N2):
                    last = nc.tensor.matmul(psM[0:1, 1, :], w3_sb[:, c:c + 1], h2T[:, c, :],
                                            start=(c == 0), stop=(c == N2 - 1))
                last.then_inc(y_done, 1)

        @block.scalar
        def _(act):
            act.wait_ge(bottomT_done, 1)
            nc.scalar.activation(bottomT[:], psT[0][:].rearrange("p b s -> p (b s)"), ACT.Copy)\
                .then_inc(bottomT_ready, 1)
            act.wait_ge(pad_ready, 1)
            act.wait_ge(weights_in, 16 * WEIGHT_DMAS)
            with nc.scalar.Fori(0, BLOCKS) as t:
                for c in range(0, len(CHUNKS), 2):
                    act.wait_ge(transposed[c], t + 1)
                    nc.scalar.activation(featT_cols(c), psT_cols(c), ACT.Copy).then_inc(featT_even, 1)
                for s in range(SPANS):
                    act.wait_ge(gram_done, SPANS * t + s + 1)
                    nc.scalar.activation(gram_to(s, 0), gram_block(s, 0), ACT.Copy)
                    nc.scalar.activation(gram_to(s, 1), gram_block(s, 1), ACT.Copy).then_inc(gram_act, 1)
                act.wait_ge(gramT_ready, t + 1)
                nc.scalar.activation(pairs_to(*KS[1]), band(*KS[1]), ACT.Copy).then_inc(pairs_act, 1)
                act.wait_ge(pairsT_done, 2 * t + 2)
                nc.scalar.activation(pairsT[:, 2, :], psM[0:ZROWS, 0, :], ACT.Copy).then_inc(pairsT_act, 1)
                for n in range(0, N1, 2):
                    act.wait_ge(h1_done, N1 * t + n + 1)
                    nc.scalar.activation(h1T[:, n, :], psG[n // 2][:, n % 2, 0:P], ACT.Relu,
                                         bias=b1_sb[:, n:n + 1]).then_inc(h1_act, 1)
                act.wait_ge(h2_done, N2 * t + 1)
                nc.scalar.activation(h2T[:, 0, :], psM[:, 0, :], ACT.Relu, bias=b2_sb[:, 0:1]).then_inc(h2_act, 1)
                act.wait_ge(y_done, t + 1)
                nc.scalar.activation(y_sb[:, bass.ts(t, P)], psM[0:1, 1, :], ACT.Copy).then_inc(y_ready, 1)

        @block.vector
        def _(dve):
            nc.vector.memset(featT[:, :, :, FEATS:Q], 0.0).then_inc(pad_ready, 1)
            dve.wait_ge(bottomT_ready, 1)
            dve.wait_ge(weights_in, 16 * WEIGHT_DMAS)
            with nc.vector.Fori(0, BLOCKS) as t:
                nc.vector.tensor_copy(featT[:, :, :, 0], bottomT[:, bass.ts(t, P)].rearrange("p (j i) -> p i j", j=NQ))\
                    .then_inc(featT_bottom, 1)
                for c in range(1, len(CHUNKS), 2):
                    dve.wait_ge(transposed[c], t + 1)
                    nc.vector.tensor_copy(featT_cols(c), psT_cols(c)).then_inc(featT_odd, 1)
                for s in range(SPANS):
                    dve.wait_ge(gram_done, SPANS * t + s + 1)
                    nc.vector.tensor_copy(gram_to(s, 2), gram_block(s, 2))
                    nc.vector.tensor_copy(gram_to(s, 3), gram_block(s, 3)).then_inc(gram_dve, 1)
                dve.wait_ge(gram_act, SPANS * t + SPANS)
                dve.wait_ge(gram_dve, SPANS * t + SPANS)
                nc.vector.transpose(gramT[:, 0:FEATS, :], gram[:].rearrange("p i g -> p g i"))
                nc.vector.transpose(gramT[:, FEATS:, :], gram[:, :, 0:KPAIR].rearrange("p i g -> p g i"))\
                    .then_inc(gramT_ready, 1)
                dve.wait_ge(gramT_ready, t + 1)
                nc.vector.tensor_copy(pairs_to(*KS[0]), band(*KS[0])).then_inc(pairs_dve, 1)
                nc.vector.tensor_copy(pairs_to(*KS[2]), band(*KS[2])).then_inc(pairs_dve, 1)
                dve.wait_ge(pairsT_done, 2 * t + 1)
                nc.vector.tensor_copy(pairsT[:, 0:2, :], psZ[0:ZROWS, 0:2, :]).then_inc(pairsT_dve, 1)
                for n in range(1, N1, 2):
                    dve.wait_ge(h1_done, N1 * t + n + 1)
                    nc.vector.tensor_scalar(h1T[:, n, :], psG[n // 2][:, n % 2, 0:P], b1_sb[:, n:n + 1], 0.0,
                                            ALU.add, ALU.max).then_inc(h1_dve, 1)
                dve.wait_ge(h2_done, N2 * t + 2)
                nc.vector.tensor_scalar(h2T[:, 1, :], psZ[:, 0, :], b2_sb[:, 1:2], 0.0, ALU.add, ALU.max)\
                    .then_inc(h2_dve, 1)


def kernel(**inputs):
    import numpy as _np
    import concourse.bacc as _bacc
    from concourse import mybir as _mybir
    from concourse.bass_utils import run_bass_kernel_spmd as _run

    x = {name: _np.ascontiguousarray(a) for name, a in inputs.items()}
    w1 = x["W_top1"]
    ids = x["ids"].reshape(BLOCKS, NQ, Q, TABLES).transpose(0, 2, 1, 3).reshape(BATCH, TABLES)
    laid = {"ids": ids, "bottom": x["r_bottom_output"]}
    for f in range(TABLES):
        laid[f"table_{f}"] = x[f"tbl_{f}"]
    laid["w1_pairs"] = w1[_np.array(pair_rows())]
    laid["w1_bottom"] = w1[PAIRS:]
    laid["b1"] = x["b_top1"].reshape(N1, P).T
    laid["w2"] = x["W_top2"]
    laid["b2"] = x["b_top2"].reshape(N2, P).T
    laid["w3"] = x["W_top3"].reshape(N2, P).T
    laid = {name: _np.ascontiguousarray(a) for name, a in laid.items()}

    nc = _bacc.Bacc("TRN2", target_bir_lowering=False, num_devices=1)
    aps = {name: nc.dram_tensor(name, a.shape, _mybir.dt.from_np(a.dtype), kind="ExternalInput").ap()
           for name, a in laid.items()}
    out = nc.dram_tensor("y", (1, BATCH), _mybir.dt.float32, kind="ExternalOutput").ap()
    build(nc, aps["ids"], aps["bottom"], [aps[f"table_{f}"] for f in range(TABLES)], aps["w1_pairs"],
          aps["w1_bottom"], aps["b1"], aps["w2"], aps["b2"], aps["w3"], out)
    r = _run(nc, [laid], core_ids=[0])
    return r.results[0]["y"].reshape(BATCH, 1)
```

```python
from contextlib import ExitStack

import concourse.bass as bass
from concourse import mybir

F32 = mybir.dt.float32
F32R = mybir.dt.float32r
I32 = mybir.dt.int32
ALU = mybir.AluOpType
ACT = mybir.ActivationFunctionType

ROWS = [1000, 125000, 1250, 1250, 1250, 1250, 1000, 1250, 1250, 1250, 12500, 1000, 12500,
        1250, 1000, 1250, 1000, 12500, 1000, 1250, 1000, 12500, 12500, 1250, 1000, 12500]
TABLES = len(ROWS)
P = 128
Q = 32
NQ = P // Q
BATCH = 512
BLOCKS = BATCH // P
D = 128
FEATS = TABLES + 1

ONEHOT = [f for f in range(TABLES) if ROWS[f] == min(ROWS)][:6]
GATHERED = [f for f in range(TABLES) if f not in ONEHOT]
VCH = 8
VROWS = min(ROWS) // VCH
ORDER = [0] + [1 + f for f in ONEHOT] + [1 + f for f in GATHERED]
DENSE = 1 + len(ONEHOT)

TPT = 4
TILES = len(GATHERED) // TPT
SPAN = P // TPT // NQ
SPANS = Q // SPAN
PART = {"a": range(0, 3), "b": range(3, TILES)}

KPAIR = (FEATS - 1) // 2
PAIRS = FEATS * KPAIR
KS = [(1, 6), (6, 10), (10, 14)]
ZCH = 3
ZROWS = PAIRS // ZCH
H1, H2 = 512, 256
N1, N2 = H1 // P, H2 // P
BANK = 512
GPB = SPAN // 2


def pair_rows():
    rows = []
    for k in range(1, KPAIR + 1):
        for f in range(FEATS):
            a, b = sorted((ORDER[f], ORDER[(f + k) % FEATS]))
            rows.append(a * FEATS - a * (a + 1) // 2 + b - a - 1)
    return rows


def build(nc, ids_gather, row_base, ids_onehot, bottom, table_rows, onehot_tables, w1_pairs, w1_bottom, b1,
          w2, b2, w3, out):
    with ExitStack() as ctx:
        def sb(name, shape, dt=F32):
            return ctx.enter_context(nc.sbuf_tensor(name, shape, dt))

        def psum(name, shape):
            return ctx.enter_context(nc.psum_tensor(name, shape, F32))

        def sem(name):
            return ctx.enter_context(nc.semaphore(name))

        NK = len(ONEHOT)
        ids_g = sb("ids_g", [P, BLOCKS * SPANS * TILES], I32)
        base_sb = sb("base_sb", [P, BLOCKS * SPANS * TILES], I32)
        rows_g = sb("rows_g", [P, BLOCKS * SPANS * TILES], I32)
        ids_o = sb("ids_o", [VROWS, NK, BATCH], I32)
        bottom_sb = sb("bottom_sb", [P, BLOCKS, D])
        w1p_sb = sb("w1p_sb", [ZROWS, ZCH, H1])
        w1b_sb = sb("w1b_sb", [P, H1])
        w2_sb = sb("w2_sb", [P, N1, H2])
        w3_sb = sb("w3_sb", [P, N2])
        b1_sb = sb("b1_sb", [P, N1])
        b2_sb = sb("b2_sb", [P, N2])
        ident = sb("ident", [P, P])
        table = sb("table", [VROWS, NK, VCH, D])
        row_i = sb("row_i", [VROWS, VCH], I32)
        row_of = sb("row_of", [VROWS, VCH])
        high = [sb(f"high{i}", [VROWS, VCH, D], F32R) for i in range(2)]
        low = [sb(f"low{i}", [VROWS, VCH, D], F32R) for i in range(2)]
        onehot = [sb(f"onehot{i}", [VROWS, VCH, BATCH], F32R) for i in range(2)]
        denseT = sb("denseT", [P, DENSE, BATCH])
        emb = sb("emb", [P, SPANS * TILES, D])
        featT = sb("featT", [P, Q, NQ, Q])
        gram = sb("gram", [P, Q, FEATS])
        gramT = sb("gramT", [P, FEATS + KPAIR, Q])
        pairs = sb("pairs", [P, PAIRS])
        pairsT = sb("pairsT", [ZROWS, ZCH, P])
        h1T = sb("h1T", [P, N1, P])
        h2T = sb("h2T", [P, N2, P])
        y_sb = sb("y_sb", [1, BATCH])

        psT = {"a": psum("psTa", [P, 4, P]), "b": psum("psTb", [P, 4, P])}
        psG = [psum(f"psG{i}", [P, 2, BANK]) for i in range(2)]
        psZ = psum("psZ", [P, 4, P])
        psM = psum("psM", [P, 4, P])

        ids_in = sem("ids_in")
        onehot_ids_in = sem("onehot_ids_in")
        other_ids_in = sem("other_ids_in")
        bottom_in = sem("bottom_in")
        weights_in = sem("weights_in")
        table_in = [sem(f"table_in{k}") for k in range(NK)]
        rows_ready = sem("rows_ready")
        ident_zero = sem("ident_zero")
        ident_ready = sem("ident_ready")
        iota_done = sem("iota_done")
        row_of_ready = sem("row_of_ready")
        pad_ready = sem("pad_ready")
        high_ready = sem("high_ready")
        low_ready = sem("low_ready")
        onehot_ready = sem("onehot_ready")
        lookup_done = sem("lookup_done")
        lookup_out = sem("lookup_out")
        bottomT_done = sem("bottomT_done")
        bottomT_ready = sem("bottomT_ready")
        gathered = [sem(f"gathered{k}") for k in range(SPANS * TILES)]
        transposed = {g: sem(f"transposed_{g}") for g in PART}
        feat_in = {g: sem(f"feat_in_{g}") for g in PART}
        dense_in = sem("dense_in")
        gram_done = sem("gram_done")
        gram_act = sem("gram_act")
        gram_dve = sem("gram_dve")
        gramT_ready = sem("gramT_ready")
        pairs_act = sem("pairs_act")
        pairs_dve = sem("pairs_dve")
        pairsT_done = sem("pairsT_done")
        pairsT_act = sem("pairsT_act")
        pairsT_dve = sem("pairsT_dve")
        h1_done = sem("h1_done")
        h1_act = sem("h1_act")
        h1_dve = sem("h1_dve")
        h2_done = sem("h2_done")
        h2_act = sem("h2_act")
        h2_dve = sem("h2_dve")
        y_done = sem("y_done")
        y_ready = sem("y_ready")
        out_written = sem("out_written")

        WEIGHT_DMAS = 6

        def gram_block(span, j):
            return psG[span % 2][Q * j:Q * (j + 1), :, 0:GPB * NQ * FEATS].rearrange(
                "p b (i s) -> p b i s", i=GPB)[:, :, :, j * FEATS:(j + 1) * FEATS]

        def gram_to(span, j):
            return gram[Q * j:Q * (j + 1), span * SPAN:(span + 1) * SPAN, :].rearrange(
                "p (b i) g -> p b i g", b=2)

        def feat_to(span, part):
            lo = DENSE + TPT * PART[part].start
            hi = DENSE + TPT * PART[part].stop
            return featT[:, span * SPAN:(span + 1) * SPAN, :, lo:hi].rearrange("p i j f -> p (i j) f")

        def feat_from(part):
            return psT[part][:, 0:len(PART[part]), :].rearrange("p q (f s) -> p s (q f)", f=TPT)

        def dense_from(t, span):
            return denseT[:, :, bass.ts(t, P)].rearrange("p f (j i) -> p i j f", j=NQ)[
                :, span * SPAN:(span + 1) * SPAN]

        def band(k0, k1):
            return bass.AP(gramT, k0 * Q, [[(FEATS + KPAIR) * Q, P], [Q, k1 - k0], [Q + 1, FEATS]])

        def pairs_to(k0, k1):
            return pairs[:, (k0 - 1) * FEATS:(k1 - 1) * FEATS].rearrange("p (k f) -> p k f", f=FEATS)

        block = ctx.enter_context(nc.Block())

        @block.sync
        def _(sp):
            sp.dma_start(ids_g[:], ids_gather).then_inc(ids_in, 16)
            sp.dma_start(base_sb[:], row_base).then_inc(ids_in, 16)
            sp.dma_start(ids_o[:, 0, :], ids_onehot[0:1, :].to_broadcast([VROWS, BATCH])).then_inc(onehot_ids_in, 16)
            for k in range(NK):
                sp.dma_start(table[:, k], onehot_tables[k].rearrange("(p c) d -> p c d", c=VCH))\
                    .then_inc(table_in[k], 16)
                if k == 0:
                    sp.dma_start(ids_o[:, 1:NK, :], ids_onehot[1:NK, :].rearrange("(o k) b -> o k b", o=1)
                                 .to_broadcast([VROWS, NK - 1, BATCH])).then_inc(other_ids_in, 16)
                    sp.dma_start(bottom_sb[:], bottom.rearrange("(t p) d -> p t d", p=P)).then_inc(bottom_in, 16)
            sp.dma_start(w1b_sb[:], w1_bottom).then_inc(weights_in, 16)
            sp.dma_start(w1p_sb[:], w1_pairs.rearrange("(c p) n -> p c n", c=ZCH)).then_inc(weights_in, 16)
            sp.dma_start(w2_sb[:], w2.rearrange("(c p) n -> p c n", c=N1)).then_inc(weights_in, 16)
            sp.dma_start(b1_sb[:], b1).then_inc(weights_in, 16)
            sp.dma_start(b2_sb[:], b2).then_inc(weights_in, 16)
            sp.dma_start(w3_sb[:], w3).then_inc(weights_in, 16)
            sp.wait_ge(y_ready, BLOCKS)
            sp.dma_start(out, y_sb[:]).then_inc(out_written, 16)
            sp.wait_ge(out_written, 16)

        @block.gpsimd
        def _(pool):
            nc.gpsimd.iota(row_i[:], pattern=[[1, VCH]], base=0, channel_multiplier=VCH).then_inc(iota_done, 1)
            nc.gpsimd.memset(ident[:], 0.0).then_inc(ident_zero, 1)
            pool.wait_ge(ident_zero, 1)
            nc.gpsimd.affine_select(out=ident[:], in_=ident[:], compare_op=ALU.not_equal, fill=1.0, base=0,
                                    pattern=[[-1, P]], channel_multiplier=1).then_inc(ident_ready, 1)
            pool.wait_ge(rows_ready, 1)
            for t in range(BLOCKS):
                for s in range(SPANS):
                    for part in PART:
                        if t > 0:
                            pool.wait_ge(transposed[part], SPANS * (t - 1) + s + 1)
                        for q in PART[part]:
                            k = s * TILES + q
                            if t > 0:
                                pool.wait_ge(gathered[k], 16 * t)
                            col = t * SPANS * TILES + k
                            nc.gpsimd.indirect_dma_start(
                                out=emb[:, k, :], out_offset=None, in_=table_rows[:],
                                in_offset=bass.IndirectOffsetOnAxis(ap=rows_g[:, col:col + 1], axis=0),
                            ).then_inc(gathered[k], 16)

        @block.tensor
        def _(pe):
            def lookup(k):
                if k >= 2:
                    pe.wait_ge(lookup_out, k - 1)
                pe.wait_ge(high_ready, k + 1)
                for c in range(VCH):
                    pe.wait_ge(onehot_ready, k * VCH + c + 1)
                    nc.tensor.matmul(psG[k % 2][:, 0, :], high[k % 2][:, c, :], onehot[k % 2][:, c, :],
                                     start=(c == 0), stop=False)
                pe.wait_ge(low_ready, k + 1)
                for c in range(VCH):
                    last = nc.tensor.matmul(psG[k % 2][:, 0, :], low[k % 2][:, c, :], onehot[k % 2][:, c, :],
                                            start=False, stop=(c == VCH - 1))
                last.then_inc(lookup_done, 1)

            def transposes(t, s, first=False):
                for part in PART:
                    if not first:
                        pe.wait_ge(feat_in[part], SPANS * t + s)
                    for n, q in enumerate(PART[part]):
                        k = s * TILES + q
                        pe.wait_ge(gathered[k], 16 * t + 16)
                        last = nc.tensor.transpose(psT[part][:, n, :], emb[:, k, :], ident[:])
                    last.then_inc(transposed[part], 1)

            def gram_products(t, s):
                for part in PART:
                    pe.wait_ge(feat_in[part], SPANS * t + s + 1)
                pe.wait_ge(dense_in, SPANS * t + s + 1)
                for n in range(SPAN):
                    i = s * SPAN + n
                    col = n % GPB * NQ * FEATS
                    last = nc.tensor.matmul(
                        psG[s % 2][:, n // GPB, col:col + NQ * FEATS],
                        featT[:, i, :, :], featT[:, i, :, 0:FEATS], start=True, stop=True)
                last.then_inc(gram_done, 1)

            def taken_out(spans):
                pe.wait_ge(gram_act, spans)
                pe.wait_ge(gram_dve, spans)

            def pair_transposes(b):
                for c in range(ZCH):
                    if c == 0:
                        pe.wait_ge(pairs_dve, 2 * b + 1)
                    elif c == 1:
                        pe.wait_ge(pairs_act, b + 1)
                    else:
                        pe.wait_ge(pairs_dve, 2 * b + 2)
                    dst = psM[0:ZROWS, 0, :] if c == 2 else psZ[0:ZROWS, c, :]
                    last = nc.tensor.transpose(dst, pairs[:, c * ZROWS:(c + 1) * ZROWS], ident[:])
                    if c > 0:
                        last.then_inc(pairsT_done, 1)

            def layer1_bottom(b, n):
                nc.tensor.matmul(psG[n // 2][:, n % 2, 0:P], w1b_sb[:, n * P:(n + 1) * P],
                                 denseT[:, 0, bass.ts(b, P)], start=True, stop=False)

            def layer1_pairs(b):
                pe.wait_ge(pairsT_dve, b + 1)
                pe.wait_ge(pairsT_act, b + 1)
                for n in range(N1):
                    for c in range(ZCH):
                        last = nc.tensor.matmul(psG[n // 2][:, n % 2, 0:P], w1p_sb[:, c, n * P:(n + 1) * P],
                                                pairsT[:, c, :], start=False, stop=(c == ZCH - 1))
                    last.then_inc(h1_done, 1)

            def layer2(b):
                for c in range(N1):
                    if c % 2 == 0:
                        pe.wait_ge(h1_act, 2 * b + c // 2 + 1)
                    else:
                        pe.wait_ge(h1_dve, 2 * b + c // 2 + 1)
                    for m in range(N2):
                        last = nc.tensor.matmul((psM if m == 0 else psZ)[:, 0, :], w2_sb[:, c, m * P:(m + 1) * P],
                                                h1T[:, c, :], start=(c == 0), stop=(c == N1 - 1))
                        if c == N1 - 1:
                            last.then_inc(h2_done, 1)

            def layer3(b):
                pe.wait_ge(h2_act, b + 1)
                pe.wait_ge(h2_dve, b + 1)
                for c in range(N2):
                    last = nc.tensor.matmul(psM[0:1, 1, :], w3_sb[:, c:c + 1], h2T[:, c, :],
                                            start=(c == 0), stop=(c == N2 - 1))
                last.then_inc(y_done, 1)

            pe.wait_ge(ident_ready, 1)
            pe.wait_ge(bottom_in, 16)
            for b in range(BLOCKS):
                last = nc.tensor.transpose(psT["b"][:, b, :], bottom_sb[:, b, :], ident[:])
            last.then_inc(bottomT_done, 1)
            for k in range(NK):
                lookup(k)
                if k == 0:
                    pe.wait_ge(bottomT_ready, 1)
                    transposes(0, 0, first=True)
                elif k in (1, 3, 4):
                    transposes(0, 1 + (1, 3, 4).index(k))
            pe.wait_ge(pad_ready, 1)
            pe.wait_ge(lookup_out, NK)
            for s in range(SPANS):
                if s >= 2:
                    taken_out(s - 1)
                gram_products(0, s)
            pe.wait_ge(weights_in, 16 * WEIGHT_DMAS)
            with nc.tensor.Fori(1, BLOCKS) as t:
                transposes(t, 0)
                taken_out(SPANS * t - 1)
                gram_products(t, 0)
                transposes(t, 1)
                pair_transposes(t - 1)
                taken_out(SPANS * t)
                gram_products(t, 1)
                transposes(t, 2)
                taken_out(SPANS * t + 2)
                for n in range(N1):
                    layer1_bottom(t - 1, n)
                layer1_pairs(t - 1)
                pe.wait_ge(h1_act, 2 * t - 1)
                pe.wait_ge(h1_dve, 2 * t - 1)
                gram_products(t, 2)
                layer2(t - 1)
                transposes(t, 3)
                layer3(t - 1)
                gram_products(t, 3)
            last_block = BLOCKS - 1
            taken_out(SPANS * BLOCKS - 1)
            layer1_bottom(last_block, 0)
            layer1_bottom(last_block, 1)
            taken_out(SPANS * BLOCKS)
            layer1_bottom(last_block, 2)
            layer1_bottom(last_block, 3)
            pair_transposes(last_block)
            layer1_pairs(last_block)
            layer2(last_block)
            layer3(last_block)

        @block.scalar
        def _(act):
            def split_high(k):
                if k >= 2:
                    act.wait_ge(lookup_done, k - 1)
                act.wait_ge(table_in[k], 16)
                nc.scalar.activation(high[k % 2][:], table[:, k], ACT.Copy).then_inc(high_ready, 1)

            def lookup_to_sbuf(k):
                act.wait_ge(lookup_done, k + 1)
                nc.scalar.activation(denseT[:, 1 + k, :], psG[k % 2][:, 0, :], ACT.Copy).then_inc(lookup_out, 1)

            def fill_dense(t, s):
                nc.scalar.activation(featT[:, s * SPAN:(s + 1) * SPAN, :, 0:DENSE], dense_from(t, s), ACT.Copy)\
                    .then_inc(dense_in, 1)

            def fill_gathered(t, s, part):
                act.wait_ge(transposed[part], SPANS * t + s + 1)
                nc.scalar.activation(feat_to(s, part), feat_from(part), ACT.Copy).then_inc(feat_in[part], 1)

            def take_gram(t, s):
                act.wait_ge(gram_done, SPANS * t + s + 1)
                nc.scalar.activation(gram_to(s, 0), gram_block(s, 0), ACT.Copy)
                nc.scalar.activation(gram_to(s, 1), gram_block(s, 1), ACT.Copy).then_inc(gram_act, 1)

            def pick_pairs(b):
                act.wait_ge(gramT_ready, b + 1)
                nc.scalar.activation(pairs_to(*KS[1]), band(*KS[1]), ACT.Copy).then_inc(pairs_act, 1)

            def pairsT_to_sbuf(b):
                act.wait_ge(pairsT_done, 2 * b + 2)
                nc.scalar.activation(pairsT[:, 2, :], psM[0:ZROWS, 0, :], ACT.Copy).then_inc(pairsT_act, 1)

            def relu1(b):
                for n in range(0, N1, 2):
                    act.wait_ge(h1_done, N1 * b + n + 1)
                    nc.scalar.activation(h1T[:, n, :], psG[n // 2][:, n % 2, 0:P], ACT.Relu,
                                         bias=b1_sb[:, n:n + 1]).then_inc(h1_act, 1)

            def relu2(b):
                act.wait_ge(h2_done, N2 * b + 1)
                nc.scalar.activation(h2T[:, 0, :], psM[:, 0, :], ACT.Relu, bias=b2_sb[:, 0:1]).then_inc(h2_act, 1)

            def y_to_sbuf(b):
                act.wait_ge(y_done, b + 1)
                nc.scalar.activation(y_sb[:, bass.ts(b, P)], psM[0:1, 1, :], ACT.Copy).then_inc(y_ready, 1)

            split_high(0)
            act.wait_ge(bottomT_done, 1)
            nc.scalar.activation(denseT[:, 0, :], psT["b"][:].rearrange("p b s -> p (b s)"), ACT.Copy)\
                .then_inc(bottomT_ready, 1)
            split_high(1)
            for k in range(NK):
                lookup_to_sbuf(k)
                if k + 2 < NK:
                    split_high(k + 2)
                if k in (0, 1, 3, 4):
                    s = (0, 1, 3, 4).index(k)
                    fill_gathered(0, s, "a")
                    fill_gathered(0, s, "b")
            act.wait_ge(lookup_out, NK)
            for s in range(SPANS):
                fill_dense(0, s)
            for s in range(SPANS):
                take_gram(0, s)
            act.wait_ge(weights_in, 16 * WEIGHT_DMAS)
            with nc.scalar.Fori(1, BLOCKS) as t:
                fill_dense(t, 0)
                fill_gathered(t, 0, "b")
                pick_pairs(t - 1)
                take_gram(t, 0)
                fill_dense(t, 1)
                fill_gathered(t, 1, "b")
                pairsT_to_sbuf(t - 1)
                take_gram(t, 1)
                fill_dense(t, 2)
                fill_gathered(t, 2, "b")
                relu1(t - 1)
                take_gram(t, 2)
                relu2(t - 1)
                fill_dense(t, 3)
                fill_gathered(t, 3, "b")
                y_to_sbuf(t - 1)
                take_gram(t, 3)
            last_block = BLOCKS - 1
            pick_pairs(last_block)
            pairsT_to_sbuf(last_block)
            relu1(last_block)
            relu2(last_block)
            y_to_sbuf(last_block)

        @block.vector
        def _(dve):
            def encode(k):
                if k == 0:
                    dve.wait_ge(onehot_ids_in, 16)
                if k == 1:
                    dve.wait_ge(other_ids_in, 16)
                if k >= 2:
                    dve.wait_ge(lookup_done, k - 1)
                for c in range(VCH):
                    nc.vector.tensor_scalar(onehot[k % 2][:, c, :], ids_o[:, k, :], row_of[:, c:c + 1], None,
                                            ALU.is_equal).then_inc(onehot_ready, 1)

            def split_low(k):
                dve.wait_ge(high_ready, k + 1)
                dve.wait_ge(table_in[k], 16)
                nc.vector.tensor_tensor(low[k % 2][:], table[:, k], high[k % 2][:].bitcast(F32), ALU.subtract)\
                    .then_inc(low_ready, 1)

            def fill_gathered(t, s, part):
                dve.wait_ge(transposed[part], SPANS * t + s + 1)
                nc.vector.tensor_copy(feat_to(s, part), feat_from(part)).then_inc(feat_in[part], 1)

            def take_gram(t, s):
                dve.wait_ge(gram_done, SPANS * t + s + 1)
                nc.vector.tensor_copy(gram_to(s, 2), gram_block(s, 2))
                nc.vector.tensor_copy(gram_to(s, 3), gram_block(s, 3)).then_inc(gram_dve, 1)

            def transpose_gram(b):
                dve.wait_ge(gram_act, SPANS * b + SPANS)
                dve.wait_ge(gram_dve, SPANS * b + SPANS)
                nc.vector.transpose(gramT[:, 0:FEATS, :], gram[:].rearrange("p i g -> p g i"))
                nc.vector.transpose(gramT[:, FEATS:, :], gram[:, :, 0:KPAIR].rearrange("p i g -> p g i"))\
                    .then_inc(gramT_ready, 1)

            def pick_pairs(b):
                dve.wait_ge(gramT_ready, b + 1)
                nc.vector.tensor_copy(pairs_to(*KS[0]), band(*KS[0])).then_inc(pairs_dve, 1)
                nc.vector.tensor_copy(pairs_to(*KS[2]), band(*KS[2])).then_inc(pairs_dve, 1)

            def pairsT_to_sbuf(b):
                dve.wait_ge(pairsT_done, 2 * b + 1)
                nc.vector.tensor_copy(pairsT[:, 0:2, :], psZ[0:ZROWS, 0:2, :]).then_inc(pairsT_dve, 1)

            def relu1(b):
                for n in range(1, N1, 2):
                    dve.wait_ge(h1_done, N1 * b + n + 1)
                    nc.vector.tensor_scalar(h1T[:, n, :], psG[n // 2][:, n % 2, 0:P], b1_sb[:, n:n + 1], 0.0,
                                            ALU.add, ALU.max).then_inc(h1_dve, 1)

            def relu2(b):
                dve.wait_ge(h2_done, N2 * b + 2)
                nc.vector.tensor_scalar(h2T[:, 1, :], psZ[:, 0, :], b2_sb[:, 1:2], 0.0, ALU.add, ALU.max)\
                    .then_inc(h2_dve, 1)

            dve.wait_ge(ids_in, 32)
            nc.vector.tensor_tensor(rows_g[:], ids_g[:], base_sb[:], ALU.add).then_inc(rows_ready, 1)
            dve.wait_ge(iota_done, 1)
            nc.vector.tensor_copy(row_of[:], row_i[:]).then_inc(row_of_ready, 1)
            dve.wait_ge(row_of_ready, 1)
            for k in range(NK):
                encode(k)
                split_low(k)
                if k == 0:
                    nc.vector.memset(featT[:, :, :, FEATS:Q], 0.0).then_inc(pad_ready, 1)
            for s in range(SPANS):
                take_gram(0, s)
            dve.wait_ge(weights_in, 16 * WEIGHT_DMAS)
            with nc.vector.Fori(1, BLOCKS) as t:
                fill_gathered(t, 0, "a")
                transpose_gram(t - 1)
                pick_pairs(t - 1)
                take_gram(t, 0)
                fill_gathered(t, 1, "a")
                pairsT_to_sbuf(t - 1)
                take_gram(t, 1)
                fill_gathered(t, 2, "a")
                relu1(t - 1)
                take_gram(t, 2)
                relu2(t - 1)
                fill_gathered(t, 3, "a")
                take_gram(t, 3)
            last_block = BLOCKS - 1
            transpose_gram(last_block)
            pick_pairs(last_block)
            pairsT_to_sbuf(last_block)
            relu1(last_block)
            relu2(last_block)


def kernel(**inputs):
    import numpy as _np
    import concourse.bacc as _bacc
    from concourse import mybir as _mybir
    from concourse.bass_utils import run_bass_kernel_spmd as _run

    x = {name: _np.ascontiguousarray(a) for name, a in inputs.items()}
    ids, w1 = x["ids"], x["W_top1"]
    ids_gather = ids[:, GATHERED].reshape(BLOCKS, NQ, SPANS, SPAN, TILES, TPT).transpose(5, 3, 1, 0, 2, 4)
    starts = _np.cumsum([0] + [ROWS[f] for f in GATHERED])[:-1].astype(ids.dtype).reshape(TILES, TPT)
    row_base = _np.broadcast_to(starts.T[:, None, None, None, None, :], ids_gather.shape)
    laid = {
        "ids_gather": ids_gather.reshape(P, -1),
        "row_base": row_base.reshape(P, -1),
        "ids_onehot": ids[:, ONEHOT].T,
        "bottom": x["r_bottom_output"],
        "table_rows": _np.concatenate([x[f"tbl_{f}"] for f in GATHERED]),
        "w1_pairs": w1[_np.array(pair_rows())],
        "w1_bottom": w1[PAIRS:],
        "b1": x["b_top1"].reshape(N1, P).T,
        "w2": x["W_top2"],
        "b2": x["b_top2"].reshape(N2, P).T,
        "w3": x["W_top3"].reshape(N2, P).T,
    }
    for f in ONEHOT:
        laid[f"table_{f}"] = x[f"tbl_{f}"]
    laid = {name: _np.ascontiguousarray(a) for name, a in laid.items()}

    nc = _bacc.Bacc("TRN2", target_bir_lowering=False, num_devices=1)
    aps = {name: nc.dram_tensor(name, a.shape, _mybir.dt.from_np(a.dtype), kind="ExternalInput").ap()
           for name, a in laid.items()}
    out = nc.dram_tensor("y", (1, BATCH), _mybir.dt.float32, kind="ExternalOutput").ap()
    build(nc, aps["ids_gather"], aps["row_base"], aps["ids_onehot"], aps["bottom"], aps["table_rows"],
          [aps[f"table_{f}"] for f in ONEHOT], aps["w1_pairs"], aps["w1_bottom"], aps["b1"], aps["w2"],
          aps["b2"], aps["w3"], out)
    r = _run(nc, [laid], core_ids=[0])
    return r.results[0]["y"].reshape(BATCH, 1)
```

```python
from contextlib import ExitStack

import concourse.bass as bass
from concourse import mybir

F32 = mybir.dt.float32
F32R = mybir.dt.float32r
I32 = mybir.dt.int32
ALU = mybir.AluOpType
ACT = mybir.ActivationFunctionType

ROWS = [1000, 125000, 1250, 1250, 1250, 1250, 1000, 1250, 1250, 1250, 12500, 1000, 12500,
        1250, 1000, 1250, 1000, 12500, 1000, 1250, 1000, 12500, 12500, 1250, 1000, 12500]
TABLES = len(ROWS)
P = 128
Q = 32
NQ = P // Q
BATCH = 512
BLOCKS = BATCH // P
D = 128
FEATS = TABLES + 1

ONEHOT = [f for f in range(TABLES) if ROWS[f] == min(ROWS)][:6]
GATHERED = [f for f in range(TABLES) if f not in ONEHOT]
VCH = 8
VROWS = min(ROWS) // VCH
ORDER = [0] + [1 + f for f in ONEHOT] + [1 + f for f in GATHERED]
ACT_CODES = 1

TPT = 4
DENSE = 1 + len(ONEHOT)
TILES = len(GATHERED) // TPT
SPAN = P // TPT // NQ
SPANS = Q // SPAN
GATHERS = SPANS * TILES
PART = {"a": range(0, TILES - TILES // 2), "b": range(TILES - TILES // 2, TILES)}

KPAIR = (FEATS - 1) // 2
PAIRS = FEATS * KPAIR
KS = [(1, 6), (6, 10), (10, 14)]
K0_G = FEATS + KS[0][1] - 1
ZCH = 3
ZROWS = PAIRS // ZCH
H1, H2 = 512, 256
N1, N2 = H1 // P, H2 // P
BANK = 512
GPB = SPAN // 2


def pair_rows():
    rows = []
    for k in range(1, KPAIR + 1):
        for f in range(FEATS):
            a, b = sorted((ORDER[f], ORDER[(f + k) % FEATS]))
            rows.append(a * FEATS - a * (a + 1) // 2 + b - a - 1)
    return rows


def build(nc, ids_and_base, ids_onehot, bottom, table_rows, onehot_tables, w1_pairs, w1_bottom, b1,
          w2, b2, w3, out):
    with ExitStack() as ctx:
        def sb(name, shape, dt=F32):
            return ctx.enter_context(nc.sbuf_tensor(name, shape, dt))

        def psum(name, shape):
            return ctx.enter_context(nc.psum_tensor(name, shape, F32))

        def sem(name):
            return ctx.enter_context(nc.semaphore(name))

        NK = len(ONEHOT)
        SPREAD_BANKS = 4
        BUFS = 3
        ids_base = sb("ids_base", [P, 2, BLOCKS * GATHERS], I32)
        rows_g = sb("rows_g", [P, BLOCKS * GATHERS], I32)
        ids_o = sb("ids_o", [NK, BATCH], I32)
        bottom_sb = sb("bottom_sb", [P, BLOCKS, D])
        w1p_sb = sb("w1p_sb", [ZROWS, ZCH, H1])
        w1b_sb = sb("w1b_sb", [P, H1])
        w2_sb = sb("w2_sb", [P, N1, H2])
        w3_sb = sb("w3_sb", [P, N2])
        b1_sb = sb("b1_sb", [P, N1])
        b2_sb = sb("b2_sb", [P, N2])
        ident = sb("ident", [P, P])
        first_ids = sb("first_ids", [VROWS, BATCH], I32)
        ids_r = sb("ids_r", [NK, BATCH], F32R)
        pick = sb("pick", [NK, NK, VROWS], F32R)
        ids_all = sb("ids_all", [VROWS, NK, BATCH])
        table = sb("table", [VROWS, NK, VCH, D])
        row_i = sb("row_i", [VROWS, VCH], I32)
        row_of = sb("row_of", [VROWS, VCH])
        minus_row = sb("minus_row", [VROWS, VCH])
        distance = sb("distance", [VROWS, BATCH])
        high = [sb(f"high{i}", [VROWS, VCH, D], F32R) for i in range(BUFS)]
        low = [sb(f"low{i}", [VROWS, VCH, D], F32R) for i in range(BUFS)]
        onehot = [sb(f"onehot{i}", [VROWS, VCH, BATCH], F32R) for i in range(BUFS)]
        denseT = sb("denseT", [P, DENSE, BATCH])
        emb = sb("emb", [P, GATHERS, D])
        featT = sb("featT", [P, Q, NQ, Q])
        gram = sb("gram", [P, Q, FEATS])
        gramT = sb("gramT", [P, FEATS + KPAIR, Q])
        pairs = sb("pairs", [P, PAIRS])
        pairsT = sb("pairsT", [ZROWS, ZCH, P])
        h1T = sb("h1T", [P, N1, P])
        h2T = sb("h2T", [P, N2, P])
        y_sb = sb("y_sb", [1, BATCH])

        psT = {"a": psum("psTa", [P, 4, P]), "b": psum("psTb", [P, 4, P])}
        psG = [psum(f"psG{i}", [P, 2, BANK]) for i in range(2)]
        psZ = psum("psZ", [P, 4, P])
        psM = psum("psM", [P, 4, P])

        ids_in = sem("ids_in")
        first_ids_in = sem("first_ids_in")
        onehot_ids_in = sem("onehot_ids_in")
        ids_r_ready = sem("ids_r_ready")
        pick_ready = sem("pick_ready")
        spread_done = sem("spread_done")
        spread_out = sem("spread_out")
        bottom_in = sem("bottom_in")
        weights_in = sem("weights_in")
        table_in = [sem(f"table_in{k}") for k in range(NK)]
        rows_ready = sem("rows_ready")
        ident_zero = sem("ident_zero")
        ident_ready = sem("ident_ready")
        iota_done = sem("iota_done")
        row_of_ready = sem("row_of_ready")
        pad_ready = sem("pad_ready")
        high_ready = sem("high_ready")
        low_ready = sem("low_ready")
        onehot_dve = sem("onehot_dve")
        onehot_act = sem("onehot_act")
        distance_ready = sem("distance_ready")
        lookup_done = sem("lookup_done")
        lookup_out = sem("lookup_out")
        bottomT_done = sem("bottomT_done")
        bottomT_ready = sem("bottomT_ready")
        gathered = [sem(f"gathered{k}") for k in range(GATHERS)]
        transposed = {g: sem(f"transposed_{g}") for g in PART}
        feat_in = {g: sem(f"feat_in_{g}") for g in PART}
        dense_in = sem("dense_in")
        gram_done = sem("gram_done")
        gram_act = sem("gram_act")
        gram_dve = sem("gram_dve")
        gramT_ready = sem("gramT_ready")
        pairs_act = sem("pairs_act")
        pairs_dve = sem("pairs_dve")
        pairsT_done = sem("pairsT_done")
        pairsT_act = sem("pairsT_act")
        pairsT_dve = sem("pairsT_dve")
        h1_done = sem("h1_done")
        h1_act = sem("h1_act")
        h1_dve = sem("h1_dve")
        h2_done = sem("h2_done")
        h2_act = sem("h2_act")
        h2_dve = sem("h2_dve")
        y_done = sem("y_done")
        y_ready = sem("y_ready")
        out_written = sem("out_written")

        WEIGHT_DMAS = 6

        def spread_psum(k):
            return (psZ[0:VROWS].rearrange("p a b -> p (a b)"), psM[0:VROWS].rearrange("p a b -> p (a b)"),
                    psG[0][0:VROWS, 1, :], psG[1][0:VROWS, 1, :])[k % SPREAD_BANKS]

        def h1_psum(n):
            return psG[1 - n // 2][:, n % 2, 0:P]

        def gram_block(span, j):
            return psG[span % 2][Q * j:Q * (j + 1), :, 0:GPB * NQ * FEATS].rearrange(
                "p b (i s) -> p b i s", i=GPB)[:, :, :, j * FEATS:(j + 1) * FEATS]

        def gram_to(span, j):
            return gram[Q * j:Q * (j + 1), span * SPAN:(span + 1) * SPAN, :].rearrange(
                "p (b i) g -> p b i g", b=2)

        def feat_to(span, part):
            lo = DENSE + TPT * PART[part].start
            hi = DENSE + TPT * PART[part].stop
            return featT[:, span * SPAN:(span + 1) * SPAN, :, lo:hi].rearrange("p i j f -> p (i j) f")

        def feat_from(part):
            return psT[part][:, 0:len(PART[part]), :].rearrange("p q (f s) -> p s (q f)", f=TPT)

        def dense_from(t, span):
            return denseT[:, :, bass.ts(t, P)].rearrange("p f (j i) -> p i j f", j=NQ)[
                :, span * SPAN:(span + 1) * SPAN]

        def band(k0, k1):
            return bass.AP(gramT, k0 * Q, [[(FEATS + KPAIR) * Q, P], [Q, k1 - k0], [Q + 1, FEATS]])

        def pairs_to(k0, k1):
            return pairs[:, (k0 - 1) * FEATS:(k1 - 1) * FEATS].rearrange("p (k f) -> p k f", f=FEATS)

        block = ctx.enter_context(nc.Block())

        @block.sync
        def _(sp):
            sp.dma_start(ids_base[:], ids_and_base).then_inc(ids_in, 16)
            sp.dma_start(first_ids[:], ids_onehot[0:1, :].to_broadcast([VROWS, BATCH])).then_inc(first_ids_in, 16)
            sp.dma_start(ids_o[:], ids_onehot).then_inc(onehot_ids_in, 16)
            for k in range(NK):
                if k >= 2:
                    sp.wait_ge(high_ready, k - 1)
                sp.dma_start(table[:, k], onehot_tables[k].rearrange("(p c) d -> p c d", c=VCH))\
                    .then_inc(table_in[k], 16)
                if k == 1:
                    sp.dma_start(bottom_sb[:], bottom.rearrange("(t p) d -> p t d", p=P)).then_inc(bottom_in, 16)
            sp.wait_ge(high_ready, NK)
            sp.dma_start(w1b_sb[:], w1_bottom).then_inc(weights_in, 16)
            sp.dma_start(w1p_sb[:], w1_pairs.rearrange("(c p) n -> p c n", c=ZCH)).then_inc(weights_in, 16)
            sp.dma_start(w2_sb[:], w2.rearrange("(c p) n -> p c n", c=N1)).then_inc(weights_in, 16)
            sp.dma_start(b1_sb[:], b1).then_inc(weights_in, 16)
            sp.dma_start(b2_sb[:], b2).then_inc(weights_in, 16)
            sp.dma_start(w3_sb[:], w3).then_inc(weights_in, 16)
            sp.wait_ge(y_ready, BLOCKS)
            sp.dma_start(out, y_sb[:]).then_inc(out_written, 16)
            sp.wait_ge(out_written, 16)

        @block.gpsimd
        def _(pool):
            nc.gpsimd.iota(row_i[:], pattern=[[1, VCH]], base=0, channel_multiplier=VCH).then_inc(iota_done, 1)
            nc.gpsimd.memset(ident[:], 0.0).then_inc(ident_zero, 1)
            pool.wait_ge(ident_zero, 1)
            nc.gpsimd.affine_select(out=ident[:], in_=ident[:], compare_op=ALU.not_equal, fill=1.0, base=0,
                                    pattern=[[-1, P]], channel_multiplier=1).then_inc(ident_ready, 1)
            pool.wait_ge(rows_ready, 1)
            def gather(t, k):
                if t > 0:
                    pool.wait_ge(gathered[k], 16 * t)
                col = t * GATHERS + k
                nc.gpsimd.indirect_dma_start(
                    out=emb[:, k, :], out_offset=None, in_=table_rows[:],
                    in_offset=bass.IndirectOffsetOnAxis(ap=rows_g[:, col:col + 1], axis=0),
                ).then_inc(gathered[k], 16)

            for t in range(BLOCKS):
                for s in range(SPANS):
                    for part in PART:
                        if t > 0:
                            pool.wait_ge(transposed[part], SPANS * (t - 1) + s + 1)
                        for q in PART[part]:
                            gather(t, s * TILES + q)

        @block.tensor
        def _(pe):
            def lookup(k):
                if k >= 2:
                    pe.wait_ge(lookup_out, k - 1)
                pe.wait_ge(high_ready, k + 1)
                for c in range(VCH):
                    if c < VCH - ACT_CODES:
                        pe.wait_ge(onehot_dve, k * (VCH - ACT_CODES) + c + 1)
                    else:
                        pe.wait_ge(onehot_act, k * ACT_CODES + c - (VCH - ACT_CODES) + 1)
                    nc.tensor.matmul(psG[k % 2][:, 0, :], high[k % BUFS][:, c, :], onehot[k % BUFS][:, c, :],
                                     start=(c == 0), stop=False)
                pe.wait_ge(low_ready, k + 1)
                for c in range(VCH):
                    last = nc.tensor.matmul(psG[k % 2][:, 0, :], low[k % BUFS][:, c, :], onehot[k % BUFS][:, c, :],
                                            start=False, stop=(c == VCH - 1))
                last.then_inc(lookup_done, 1)

            def transposes(t, s, first=False):
                for part in PART:
                    if not first:
                        pe.wait_ge(feat_in[part], SPANS * t + s)
                    for n, q in enumerate(PART[part]):
                        k = s * TILES + q
                        pe.wait_ge(gathered[k], 16 * t + 16)
                        last = nc.tensor.transpose(psT[part][:, n, :], emb[:, k, :], ident[:])
                    last.then_inc(transposed[part], 1)

            def gram_products(t, s):
                for part in PART:
                    pe.wait_ge(feat_in[part], SPANS * t + s + 1)
                pe.wait_ge(dense_in, SPANS * t + s + 1)
                for n in range(SPAN):
                    i = s * SPAN + n
                    col = n % GPB * NQ * FEATS
                    last = nc.tensor.matmul(
                        psG[s % 2][:, n // GPB, col:col + NQ * FEATS],
                        featT[:, i, :, :], featT[:, i, :, 0:FEATS], start=True, stop=True)
                    if n % GPB == GPB - 1:
                        last.then_inc(gram_done, 1)

            def taken_out(spans):
                pe.wait_ge(gram_act, spans)
                pe.wait_ge(gram_dve, spans)

            def pair_transposes(b):
                for c in range(ZCH):
                    if c == 0:
                        pe.wait_ge(pairs_act, b + 1)
                    else:
                        pe.wait_ge(pairs_dve, 2 * b + c)
                    dst = psZ[0:ZROWS, 0, :] if c == 0 else psM[0:ZROWS, 1 + c, :]
                    last = nc.tensor.transpose(dst, pairs[:, c * ZROWS:(c + 1) * ZROWS], ident[:])
                    if c != 1:
                        last.then_inc(pairsT_done, 1)

            def layer1_bottom(b, n):
                nc.tensor.matmul(h1_psum(n), w1b_sb[:, n * P:(n + 1) * P],
                                 denseT[:, 0, bass.ts(b, P)], start=True, stop=False)

            def layer1_pairs(b, parts):
                pe.wait_ge(pairsT_act, b + 1)
                for n in parts:
                    nc.tensor.matmul(h1_psum(n), w1p_sb[:, 0, n * P:(n + 1) * P],
                                     pairsT[:, 0, :], start=False, stop=False)
                pe.wait_ge(pairsT_dve, b + 1)
                for n in parts:
                    for c in range(1, ZCH):
                        last = nc.tensor.matmul(h1_psum(n), w1p_sb[:, c, n * P:(n + 1) * P],
                                                pairsT[:, c, :], start=False, stop=(c == ZCH - 1))
                    last.then_inc(h1_done, 1)

            def layer2(b):
                for c in range(N1):
                    if c % 2 == 0:
                        pe.wait_ge(h1_act, 2 * b + c // 2 + 1)
                    else:
                        pe.wait_ge(h1_dve, 2 * b + c // 2 + 1)
                    for m in range(N2):
                        last = nc.tensor.matmul((psM if m == 0 else psZ)[:, 0, :], w2_sb[:, c, m * P:(m + 1) * P],
                                                h1T[:, c, :], start=(c == 0), stop=(c == N1 - 1))
                        if c == N1 - 1:
                            last.then_inc(h2_done, 1)

            def layer3(b):
                for c in range(N2):
                    pe.wait_ge(h2_act if c == 0 else h2_dve, b + 1)
                    last = nc.tensor.matmul(psM[0:1, 1, :], w3_sb[:, c:c + 1], h2T[:, c, :],
                                            start=(c == 0), stop=(c == N2 - 1))
                last.then_inc(y_done, 1)

            pe.wait_ge(ids_r_ready, 1)
            pe.wait_ge(pick_ready, 1)
            def spread(k):
                if k > SPREAD_BANKS:
                    pe.wait_ge(spread_out, k - SPREAD_BANKS)
                nc.tensor.matmul(spread_psum(k), pick[:, k, :], ids_r[:], start=True, stop=True)\
                    .then_inc(spread_done, 1)

            for k in range(1, 1 + SPREAD_BANKS):
                spread(k)
            for k in range(NK):
                lookup(k)
                if k == 0:
                    for later in range(1 + SPREAD_BANKS, NK):
                        spread(later)
                    pe.wait_ge(bottom_in, 16)
                    pe.wait_ge(ident_ready, 1)
                    for b in range(BLOCKS):
                        last = nc.tensor.transpose(psT["b"][:, b, :], bottom_sb[:, b, :], ident[:])
                    last.then_inc(bottomT_done, 1)
                elif k == 1:
                    pe.wait_ge(bottomT_ready, 1)
                elif k <= SPANS + 1:
                    transposes(0, k - 2, first=(k == 2))
            pe.wait_ge(pad_ready, 1)
            pe.wait_ge(lookup_out, NK - 1)
            gram_products(0, 0)
            pe.wait_ge(lookup_out, NK)
            gram_products(0, 1)
            taken_out(1)
            gram_products(0, 2)
            transposes(1, 0)
            taken_out(2)
            gram_products(0, 3)
            pe.wait_ge(weights_in, 16 * WEIGHT_DMAS)

            def layer1(b, half):
                for n in (2 * half, 2 * half + 1):
                    layer1_bottom(b, n)
                layer1_pairs(b, (2 * half, 2 * half + 1))

            def h1_taken(halves):
                pe.wait_ge(h1_act, halves)
                pe.wait_ge(h1_dve, halves)

            with nc.tensor.Fori(1, BLOCKS - 1) as t:
                taken_out(SPANS * t - 1)
                gram_products(t, 0)
                transposes(t, 1)
                pair_transposes(t - 1)
                taken_out(SPANS * t)
                layer1(t - 1, 0)
                taken_out(SPANS * t + 1)
                layer1(t - 1, 1)
                transposes(t, 2)
                h1_taken(2 * t - 1)
                gram_products(t, 1)
                h1_taken(2 * t)
                gram_products(t, 2)
                transposes(t, 3)
                layer2(t - 1)
                taken_out(SPANS * t + 2)
                gram_products(t, 3)
                transposes(t + 1, 0)
                layer3(t - 1)

            t = BLOCKS - 1
            taken_out(SPANS * t - 1)
            gram_products(t, 0)
            pair_transposes(t - 1)
            taken_out(SPANS * t)
            layer1(t - 1, 0)
            transposes(t, 1)
            taken_out(SPANS * t + 1)
            layer1(t - 1, 1)
            h1_taken(2 * t - 1)
            gram_products(t, 1)
            transposes(t, 2)
            layer2(t - 1)
            layer3(t - 1)
            gram_products(t, 2)
            taken_out(SPANS * t + 2)
            transposes(t, 3)
            gram_products(t, 3)
            last_block = BLOCKS - 1
            taken_out(SPANS * BLOCKS - 1)
            layer1_bottom(last_block, 2)
            layer1_bottom(last_block, 3)
            taken_out(SPANS * BLOCKS)
            layer1_bottom(last_block, 0)
            layer1_bottom(last_block, 1)
            pe.wait_ge(y_ready, last_block)
            pair_transposes(last_block)
            layer1_pairs(last_block, range(N1))
            layer2(last_block)
            layer3(last_block)

        @block.scalar
        def _(act):
            def split_high(k):
                if k >= BUFS:
                    act.wait_ge(lookup_done, k - BUFS + 1)
                act.wait_ge(table_in[k], 16)
                nc.scalar.activation(high[k % BUFS][:], table[:, k], ACT.Copy).then_inc(high_ready, 1)

            def lookup_to_sbuf(k):
                act.wait_ge(lookup_done, k + 1)
                nc.scalar.activation(denseT[:, 1 + k, :], psG[k % 2][:, 0, :], ACT.Copy).then_inc(lookup_out, 1)

            def encode(k):
                act.wait_ge(row_of_ready, 2)
                if k == 0:
                    act.wait_ge(first_ids_in, 16)
                else:
                    act.wait_ge(spread_out, k)
                source = first_ids[:] if k == 0 else ids_all[:, k, :]
                for n in range(ACT_CODES):
                    c = VCH - ACT_CODES + n
                    if k + n > 0:
                        act.wait_ge(onehot_act, k * ACT_CODES + n)
                    nc.scalar.activation(distance[:], source, ACT.Abs, bias=minus_row[:, c:c + 1])\
                        .then_inc(distance_ready, 1)
                    act.wait_ge(distance_ready, k * ACT_CODES + n + 1)
                    nc.scalar.activation(onehot[k % BUFS][:, c, :], distance[:], ACT.Relu, scale=-1.0, bias=1.0)\
                        .then_inc(onehot_act, 1)

            def fill_dense(t, s):
                nc.scalar.activation(featT[:, s * SPAN:(s + 1) * SPAN, :, 0:DENSE], dense_from(t, s), ACT.Copy)\
                    .then_inc(dense_in, 1)

            def first_block_dense():
                act.wait_ge(lookup_out, NK - 1)
                act.wait_ge(bottomT_ready, 1)
                for s in range(SPANS):
                    nc.scalar.activation(featT[:, s * SPAN:(s + 1) * SPAN, :, 0:DENSE - 1],
                                         dense_from(0, s)[:, :, :, 0:DENSE - 1], ACT.Copy)
                act.wait_ge(lookup_done, NK)
                nc.scalar.activation(featT[:, :, :, DENSE - 1].rearrange("p i j -> p j i"),
                                     psG[(NK - 1) % 2][:, 0, 0:P].rearrange("p (j i) -> p j i", j=NQ),
                                     ACT.Copy).then_inc(dense_in, SPANS)

            def fill_gathered(t, s, part):
                act.wait_ge(transposed[part], SPANS * t + s + 1)
                nc.scalar.activation(feat_to(s, part), feat_from(part), ACT.Copy).then_inc(feat_in[part], 1)

            def take_gram(t, s):
                act.wait_ge(gram_done, 2 * (SPANS * t + s + 1))
                nc.scalar.activation(gram_to(s, 0), gram_block(s, 0), ACT.Copy)
                nc.scalar.activation(gram_to(s, 1), gram_block(s, 1), ACT.Copy).then_inc(gram_act, 1)

            def take_gram_halves(t, s):
                for h in range(2):
                    act.wait_ge(gram_done, 2 * (SPANS * t + s) + h + 1)
                    nc.scalar.activation(gram_to(s, 0)[:, h], gram_block(s, 0)[:, h], ACT.Copy)
                    last = nc.scalar.activation(gram_to(s, 1)[:, h], gram_block(s, 1)[:, h], ACT.Copy)
                last.then_inc(gram_act, 1)

            def pick_pairs(b):
                act.wait_ge(gramT_ready, 2 * b + 1)
                nc.scalar.activation(pairs_to(*KS[0]), band(*KS[0]), ACT.Copy).then_inc(pairs_act, 1)

            def pairsT_to_sbuf(b):
                act.wait_ge(pairsT_done, 2 * b + 1)
                nc.scalar.activation(pairsT[:, 0, :], psZ[0:ZROWS, 0, :], ACT.Copy).then_inc(pairsT_act, 1)

            def relu1(b, half):
                act.wait_ge(h1_done, N1 * b + 2 * half + 1)
                nc.scalar.activation(h1T[:, 2 * half, :], h1_psum(2 * half), ACT.Relu,
                                     bias=b1_sb[:, 2 * half:2 * half + 1]).then_inc(h1_act, 1)

            def relu2(b):
                act.wait_ge(h2_done, N2 * b + 1)
                nc.scalar.activation(h2T[:, 0, :], psM[:, 0, :], ACT.Relu, bias=b2_sb[:, 0:1]).then_inc(h2_act, 1)

            def y_to_sbuf(b):
                act.wait_ge(y_done, b + 1)
                nc.scalar.activation(y_sb[:, bass.ts(b, P)], psM[0:1, 1, :], ACT.Copy).then_inc(y_ready, 1)

            def spread_to_sbuf(k):
                act.wait_ge(spread_done, k)
                nc.scalar.activation(ids_all[:, k, :], spread_psum(k), ACT.Copy).then_inc(spread_out, 1)

            act.wait_ge(ident_ready, 1)
            nc.scalar.activation(pick[:], ident[0:NK, 0:NK].unsqueeze(2).to_broadcast([NK, NK, VROWS]), ACT.Copy)\
                .then_inc(pick_ready, 1)
            spread_to_sbuf(1)
            spread_to_sbuf(2)
            split_high(0)
            encode(0)
            spread_to_sbuf(3)
            split_high(1)
            encode(1)
            spread_to_sbuf(4)
            split_high(2)
            encode(2)
            for k in range(NK):
                if k == NK - 1:
                    first_block_dense()
                lookup_to_sbuf(k)
                if k == 0:
                    for later in range(5, NK):
                        spread_to_sbuf(later)
                if k + 3 < NK:
                    split_high(k + 3)
                    encode(k + 3)
                if k == 0:
                    act.wait_ge(bottomT_done, 1)
                    nc.scalar.activation(denseT[:, 0, :], psT["b"][:].rearrange("p b s -> p (b s)"), ACT.Copy)\
                        .then_inc(bottomT_ready, 1)
                elif 2 <= k <= SPANS + 1:
                    fill_gathered(0, k - 2, "a")
                    fill_gathered(0, k - 2, "b")
            act.wait_ge(lookup_out, NK)
            take_gram(0, 0)
            fill_dense(1, 0)
            take_gram(0, 1)
            fill_dense(1, 1)
            take_gram(0, 2)
            fill_gathered(1, 0, "b")
            fill_dense(1, 2)
            take_gram(0, 3)
            pick_pairs(0)
            fill_dense(1, 3)
            act.wait_ge(weights_in, 16 * WEIGHT_DMAS)

            with nc.scalar.Fori(1, BLOCKS - 1) as t:
                act.wait_ge(gramT_ready, 2 * t)
                take_gram(t, 0)
                pairsT_to_sbuf(t - 1)
                fill_gathered(t, 1, "b")
                fill_dense(t + 1, 0)
                relu1(t - 1, 0)
                relu1(t - 1, 1)
                fill_gathered(t, 2, "b")
                take_gram(t, 1)
                fill_dense(t + 1, 1)
                take_gram(t, 2)
                fill_gathered(t, 3, "b")
                fill_dense(t + 1, 2)
                relu2(t - 1)
                take_gram(t, 3)
                fill_gathered(t + 1, 0, "b")
                y_to_sbuf(t - 1)
                pick_pairs(t)
                fill_dense(t + 1, 3)

            t = BLOCKS - 1
            act.wait_ge(gramT_ready, 2 * t)
            take_gram(t, 0)
            pairsT_to_sbuf(t - 1)
            relu1(t - 1, 0)
            fill_gathered(t, 1, "b")
            relu1(t - 1, 1)
            take_gram(t, 1)
            fill_gathered(t, 2, "b")
            relu2(t - 1)
            y_to_sbuf(t - 1)
            take_gram(t, 2)
            fill_gathered(t, 3, "b")
            take_gram_halves(t, 3)
            pick_pairs(t)
            last_block = BLOCKS - 1
            pairsT_to_sbuf(last_block)
            relu1(last_block, 0)
            relu1(last_block, 1)
            relu2(last_block)
            y_to_sbuf(last_block)

        @block.vector
        def _(dve):
            def encode(k):
                if k == 0:
                    dve.wait_ge(first_ids_in, 16)
                else:
                    dve.wait_ge(spread_out, k)
                if k >= BUFS:
                    dve.wait_ge(lookup_done, k - BUFS + 1)
                source = first_ids[:] if k == 0 else ids_all[:, k, :]
                for c in range(VCH - ACT_CODES):
                    nc.vector.tensor_scalar(onehot[k % BUFS][:, c, :], source, row_of[:, c:c + 1], None,
                                            ALU.is_equal).then_inc(onehot_dve, 1)

            def split_low(k):
                dve.wait_ge(high_ready, k + 1)
                dve.wait_ge(table_in[k], 16)
                nc.vector.tensor_tensor(low[k % BUFS][:], table[:, k], high[k % BUFS][:].bitcast(F32), ALU.subtract)\
                    .then_inc(low_ready, 1)

            def fill_gathered(t, s, part):
                dve.wait_ge(transposed[part], SPANS * t + s + 1)
                nc.vector.tensor_copy(feat_to(s, part), feat_from(part)).then_inc(feat_in[part], 1)

            def take_gram(t, s):
                dve.wait_ge(gram_done, 2 * (SPANS * t + s + 1))
                nc.vector.tensor_copy(gram_to(s, 2), gram_block(s, 2))
                nc.vector.tensor_copy(gram_to(s, 3), gram_block(s, 3)).then_inc(gram_dve, 1)

            def take_gram_halves(t, s):
                for h in range(2):
                    dve.wait_ge(gram_done, 2 * (SPANS * t + s) + h + 1)
                    nc.vector.tensor_copy(gram_to(s, 2)[:, h], gram_block(s, 2)[:, h])
                    last = nc.vector.tensor_copy(gram_to(s, 3)[:, h], gram_block(s, 3)[:, h])
                last.then_inc(gram_dve, 1)

            def transpose_gram(b):
                dve.wait_ge(gram_act, SPANS * b + SPANS)
                dve.wait_ge(gram_dve, SPANS * b + SPANS)
                again = K0_G - FEATS
                nc.vector.transpose(gramT[:, 0:FEATS, :], gram[:].rearrange("p i g -> p g i"))
                nc.vector.transpose(gramT[:, FEATS:K0_G, :], gram[:, :, 0:again].rearrange("p i g -> p g i"))\
                    .then_inc(gramT_ready, 1)
                nc.vector.transpose(gramT[:, K0_G:, :], gram[:, :, again:KPAIR].rearrange("p i g -> p g i"))\
                    .then_inc(gramT_ready, 1)

            def pick_pairs(b):
                dve.wait_ge(gramT_ready, 2 * b + 2)
                nc.vector.tensor_copy(pairs_to(*KS[1]), band(*KS[1])).then_inc(pairs_dve, 1)
                nc.vector.tensor_copy(pairs_to(*KS[2]), band(*KS[2])).then_inc(pairs_dve, 1)

            def pairsT_to_sbuf(b):
                dve.wait_ge(pairsT_done, 2 * b + 2)
                nc.vector.tensor_copy(pairsT[:, 1:3, :], psM[0:ZROWS, 2:4, :]).then_inc(pairsT_dve, 1)

            def relu2(b):
                dve.wait_ge(h2_done, N2 * b + 2)
                nc.vector.tensor_scalar(h2T[:, 1, :], psZ[:, 0, :], b2_sb[:, 1:2], 0.0, ALU.add, ALU.max)\
                    .then_inc(h2_dve, 1)

            def relu1(b, half):
                n = 2 * half + 1
                dve.wait_ge(h1_done, N1 * b + n + 1)
                nc.vector.tensor_scalar(h1T[:, n, :], h1_psum(n), b1_sb[:, n:n + 1], 0.0,
                                        ALU.add, ALU.max).then_inc(h1_dve, 1)

            dve.wait_ge(iota_done, 1)
            nc.vector.tensor_copy(row_of[:], row_i[:]).then_inc(row_of_ready, 1)
            nc.vector.tensor_scalar(minus_row[:], row_i[:], -1.0, None, ALU.mult).then_inc(row_of_ready, 1)
            dve.wait_ge(row_of_ready, 2)
            dve.wait_ge(ids_in, 16)
            nc.vector.tensor_tensor(rows_g[:], ids_base[:, 0, :], ids_base[:, 1, :], ALU.add).then_inc(rows_ready, 1)
            dve.wait_ge(onehot_ids_in, 16)
            nc.vector.tensor_copy(ids_r[:], ids_o[:]).then_inc(ids_r_ready, 1)
            for k in range(NK):
                encode(k)
                split_low(k)
                if k == 0:
                    nc.vector.memset(featT[:, :, :, FEATS:Q], 0.0).then_inc(pad_ready, 1)
            take_gram(0, 0)
            take_gram(0, 1)
            take_gram(0, 2)
            fill_gathered(1, 0, "a")
            take_gram(0, 3)
            transpose_gram(0)
            pick_pairs(0)
            dve.wait_ge(weights_in, 16 * WEIGHT_DMAS)

            with nc.vector.Fori(1, BLOCKS - 1) as t:
                take_gram(t, 0)
                pairsT_to_sbuf(t - 1)
                fill_gathered(t, 1, "a")
                relu1(t - 1, 0)
                relu1(t - 1, 1)
                fill_gathered(t, 2, "a")
                take_gram(t, 1)
                take_gram(t, 2)
                fill_gathered(t, 3, "a")
                relu2(t - 1)
                take_gram(t, 3)
                fill_gathered(t + 1, 0, "a")
                transpose_gram(t)
                pick_pairs(t)

            t = BLOCKS - 1
            take_gram(t, 0)
            pairsT_to_sbuf(t - 1)
            relu1(t - 1, 0)
            fill_gathered(t, 1, "a")
            relu1(t - 1, 1)
            take_gram(t, 1)
            fill_gathered(t, 2, "a")
            relu2(t - 1)
            take_gram(t, 2)
            fill_gathered(t, 3, "a")
            take_gram_halves(t, 3)
            transpose_gram(t)
            pick_pairs(t)
            last_block = BLOCKS - 1
            pairsT_to_sbuf(last_block)
            relu1(last_block, 0)
            relu1(last_block, 1)
            relu2(last_block)


def kernel(**inputs):
    import numpy as _np
    import concourse.bacc as _bacc
    from concourse import mybir as _mybir
    from concourse.bass_utils import run_bass_kernel_spmd as _run

    x = {name: _np.ascontiguousarray(a) for name, a in inputs.items()}
    ids, w1 = x["ids"], x["W_top1"]
    tiles = ids[:, GATHERED].reshape(BLOCKS, NQ, SPANS, SPAN, TILES, TPT).transpose(5, 3, 1, 0, 2, 4)
    starts = _np.cumsum([0] + [ROWS[f] for f in GATHERED])[:-1].astype(ids.dtype)
    base = _np.broadcast_to(starts.reshape(TILES, TPT).T[:, None, None, None, None, :], tiles.shape)
    laid = {
        "ids_and_base": _np.stack([tiles.reshape(P, -1), base.reshape(P, -1)], axis=1),
        "ids_onehot": ids[:, ONEHOT].T,
        "bottom": x["r_bottom_output"],
        "table_rows": _np.concatenate([x[f"tbl_{f}"] for f in GATHERED]),
        "w1_pairs": w1[_np.array(pair_rows())],
        "w1_bottom": w1[PAIRS:],
        "b1": x["b_top1"].reshape(N1, P).T,
        "w2": x["W_top2"],
        "b2": x["b_top2"].reshape(N2, P).T,
        "w3": x["W_top3"].reshape(N2, P).T,
    }
    for f in ONEHOT:
        laid[f"table_{f}"] = x[f"tbl_{f}"]
    laid = {name: _np.ascontiguousarray(a) for name, a in laid.items()}

    nc = _bacc.Bacc("TRN2", target_bir_lowering=False, num_devices=1)
    aps = {name: nc.dram_tensor(name, a.shape, _mybir.dt.from_np(a.dtype), kind="ExternalInput").ap()
           for name, a in laid.items()}
    out = nc.dram_tensor("y", (1, BATCH), _mybir.dt.float32, kind="ExternalOutput").ap()
    build(nc, aps["ids_and_base"], aps["ids_onehot"], aps["bottom"], aps["table_rows"],
          [aps[f"table_{f}"] for f in ONEHOT], aps["w1_pairs"], aps["w1_bottom"], aps["b1"], aps["w2"],
          aps["b2"], aps["w3"], out)
    r = _run(nc, [laid], core_ids=[0])
    return r.results[0]["y"].reshape(BATCH, 1)
```
